# Optimizing a Trainium2 kernel written in Bass

```python
import numpy as np
import jax
import jax.numpy as jnp

def _softmax(x, axis=-1):
    return jax.nn.softmax(x, axis=axis)

def _gelu(x):
    return jax.nn.gelu(x, approximate=True)

def _silu(x):
    return jax.nn.silu(x)

def _sigmoid(x):
    return jax.nn.sigmoid(x)

def _layernorm(x, axis=-1, eps=1e-05):
    m = jnp.mean(x, axis=axis, keepdims=True)
    v = jnp.var(x, axis=axis, keepdims=True)
    return (x - m) / jnp.sqrt(v + eps)

def _scatter_add(tgt, idx, src, axis=0):
    return tgt.at[idx].add(src)

def _segment_sum(src, seg, n):
    return jax.ops.segment_sum(src, seg, n)
kernel_name = 'mk_adj_preln_d1_adj_r2_1578a3'

def setup_inputs(seed: int=0):
    np.random.seed(seed)
    _w = jnp.asarray

    def _rec_inputs():
        import jax
        import jax.numpy as jnp
        _gk = jax.random.key(seed)
        x = 0.0001732 + 1 * jax.random.normal(jax.random.fold_in(_gk, 1), (5120, 64), jnp.float32)
        _a = jax.random.bernoulli(jax.random.fold_in(_gk, 2), 0.00078125, (5120, 5120))
        _a = jnp.logical_or(_a, jnp.swapaxes(_a, -1, -2))
        _a = jnp.logical_or(_a, jnp.eye(5120, dtype=bool))
        _af = _a.astype(jnp.float32)
        _af = _af * jax.random.uniform(jax.random.fold_in(_gk, 3), (5120, 5120), jnp.float32, 0.05, 0.02)
        adj = _af
        return (x, adj)
    x, adj = _rec_inputs()

    def _L0_gnn_setup():
        import jax, jax.numpy as jnp
        import numpy as np
        N_USERS = 2048
        N_ITEMS = 3072
        EMB = 64
        LN_EPS = 1e-05
        key = jax.random.key(seed)
        ks = jax.random.split(key, 10)
        N = N_USERS + N_ITEMS
        ego = jax.random.normal(ks[0], (N, EMB), jnp.float32)
        adj = (jax.random.uniform(ks[1], (N, N), jnp.float32) < 0.01).astype(jnp.float32) * 0.02
        xav = float(np.sqrt(6.0 / (EMB + EMB)))
        W_u = jax.random.uniform(ks[2], (EMB, EMB), jnp.float32, -xav, xav)
        W_i = jax.random.uniform(ks[3], (EMB, EMB), jnp.float32, -xav, xav)
        diag_u = jax.random.uniform(ks[4], (N_USERS,), jnp.float32, 0.99, 1.01)
        diag_i = jax.random.uniform(ks[5], (N_ITEMS,), jnp.float32, 0.99, 1.01)
        par_u = jax.random.uniform(ks[6], (2,), jnp.float32, 0.0, 0.99)
        par_i = jax.random.uniform(ks[7], (2,), jnp.float32, 0.0, 0.99)
        ln_gamma = jnp.ones((EMB,), jnp.float32)
        ln_beta = jnp.zeros((EMB,), jnp.float32)
        return {'ego_embeddings': ego, 'adj': adj, 'W_u': W_u, 'diag_u': diag_u, 'par_u': par_u, 'W_i': W_i, 'diag_i': diag_i, 'par_i': par_i, 'ln_gamma': ln_gamma, 'ln_beta': ln_beta}
    _L0_gnn_all = _L0_gnn_setup()
    _L0_gnn_in = {k: v for k, v in _L0_gnn_all.items() if k in ('W_u', 'diag_u', 'par_u', 'W_i', 'diag_i', 'par_i', 'ln_gamma', 'ln_beta')}
    del _L0_gnn_all
    return {'x': x, 'adj': adj, 'L0_gnn_W_u': _L0_gnn_in['W_u'], 'L0_gnn_diag_u': _L0_gnn_in['diag_u'], 'L0_gnn_par_u': _L0_gnn_in['par_u'], 'L0_gnn_W_i': _L0_gnn_in['W_i'], 'L0_gnn_diag_i': _L0_gnn_in['diag_i'], 'L0_gnn_par_i': _L0_gnn_in['par_i'], 'L0_gnn_ln_gamma': _L0_gnn_in['ln_gamma'], 'L0_gnn_ln_beta': _L0_gnn_in['ln_beta']}

def reference(x, adj, L0_gnn_W_u, L0_gnn_diag_u, L0_gnn_par_u, L0_gnn_W_i, L0_gnn_diag_i, L0_gnn_par_i, L0_gnn_ln_gamma, L0_gnn_ln_beta):
    import jax
    import jax.numpy as jnp

    def _L0_gnn_ref(ego_embeddings, adj, W_u, diag_u, par_u, W_i, diag_i, par_i, ln_gamma, ln_beta):
        import jax, jax.numpy as jnp
        import numpy as np
        N_USERS = 2048
        N_ITEMS = 3072
        EMB = 64
        LN_EPS = 1e-05
        nu = diag_u.shape[0]
        res = ego_embeddings
        ego_u = ego_embeddings[:nu]
        ego_i = ego_embeddings[nu:]
        u = par_u[0] * par_u[1] * (diag_u[:, None] * ego_u @ W_u) + ego_u
        i = par_i[0] * par_i[1] * (diag_i[:, None] * ego_i @ W_i) + ego_i
        e = jnp.concatenate([u, i], axis=0)
        h = adj @ (adj.T @ e)
        mu = jnp.mean(h, axis=-1, keepdims=True)
        var = jnp.var(h, axis=-1, keepdims=True)
        out = (h - mu) * jax.lax.rsqrt(var + LN_EPS) * ln_gamma + ln_beta + res
        return out
    h = jnp.maximum(_layernorm(x, axis=-1), 0.0)
    x = x + _L0_gnn_ref(h, adj, L0_gnn_W_u, L0_gnn_diag_u, L0_gnn_par_u, L0_gnn_W_i, L0_gnn_diag_i, L0_gnn_par_i, L0_gnn_ln_gamma, L0_gnn_ln_beta)
    return x

_drawn_inputs = setup_inputs


def setup_inputs(seed=0):
    import zlib

    import numpy as np

    out = dict(_drawn_inputs(seed))
    spreads = {'L0_gnn_ln_gamma': (1.0, 0.2), 'L0_gnn_ln_beta': (0.0, 0.1)}
    factors = {}
    for name, (base, spread) in spreads.items():
        noise = np.random.default_rng([zlib.crc32(name.encode()), seed]).standard_normal(out[name].shape)
        drawn = base * np.exp(spread * noise) if base else spread * noise
        out[name] = jnp.asarray(drawn.astype(out[name].dtype))
    for name, factor in factors.items():
        out[name] = (out[name] * factor).astype(out[name].dtype)
    return out
```

```python
from contextlib import ExitStack

import concourse.bass as bass
from concourse import mybir

F32 = mybir.dt.float32
U32 = mybir.dt.uint32
ALU = mybir.AluOpType
ACT = mybir.ActivationFunctionType
AX_X = mybir.AxisListType.X

P = 128
EPS = 1e-5

G = 4
SQ = 32


def build(nc, x, adj, W_u, diag_u, par_u, W_i, diag_i, par_i, ln_gamma, ln_beta, out):
    N, D = x.shape
    T = N // P
    NU = diag_u.shape[0]
    RUN = N // G
    HALF = RUN // 2
    XB = HALF // P
    QB = P // SQ
    J = RUN // SQ
    A = P // SQ
    assert G * RUN == N and XB * P == HALF and 2 * D == P and XB == 5

    CACHED = 5
    STREAMED = T - CACHED
    ITER = T // CACHED
    CACHE_AT = 3
    SLOTS = 4
    assert ITER * CACHED == T and ITER % SLOTS == 0
    CG = J // 4

    PLAN = [("cached", 0), ("cached", 1), ("pairs", 0, 6), ("cached", 2), ("cached", 3), ("pairs", 12, 6),
            ("cached", 4), ("pairs", 24, 5), ("single", STREAMED - 1)]
    ORDER = []
    for step in PLAN:
        if step[0] == "cached":
            ORDER.append(STREAMED + step[1])
        elif step[0] == "single":
            ORDER.append(step[1])
        else:
            ORDER += range(step[1], step[1] + 2 * step[2])
    assert sorted(ORDER) == list(range(T))

    with ExitStack() as ctx:
        def sb(name, shape, dt=F32):
            return ctx.enter_context(nc.sbuf_tensor(name, shape, dt))

        def bank(name):
            return ctx.enter_context(nc.psum_tensor(name, [P, 512], F32))

        def sem(name):
            return ctx.enter_context(nc.semaphore(name))

        work = sb("work", [P, SLOTS, N])
        cache = sb("cache", [P, CACHED, J, P])
        hv = sb("hv", [P, T, D])
        xr = sb("xr", [P, T, D])
        ident = sb("ident", [P, P])
        center = sb("center", [P, D])
        w_both = sb("w_both", [P, D])
        par = sb("par", [P, 2])
        diag = sb("diag", [P, 2, T])
        gamma = sb("gamma", [P, D])
        beta = sb("beta", [P, D])
        scaled = sb("scaled", [P, 2, 2, D])
        scaled_t = sb("scaled_t", [P, 2, P])
        e_tile = sb("e_tile", [P, 2, D])
        stat = sb("stat", [P, 3, T])
        square = sb("square", [P, D])
        h_t = sb("h_t", [P, 2, P])
        ssq = sb("ssq", [P, 2])
        std = sb("std", [P, 2])
        rstd = sb("rstd", [P, 2])
        z = sb("z", [P, 2, D])
        eps = sb("eps", [P, 1])
        two_tiles = sb("two_tiles", [P, A], U32)
        run_at = sb("run_at", [P, 2, A], U32)

        turned = work[:, 0:2, :].rearrange("p b (j r) -> p b j r", r=P)
        gathered = work[:, 2:4, :].rearrange("p b (a c) -> p b a c", a=A)
        vt = work[:, 1, 0:XB * 512].rearrange("p (b q g c) -> p b q g c", b=XB, q=QB, g=G)
        v = hv[:].rearrange("p t d -> p (t d)").rearrange("p (b q h d) -> p b q h d", b=XB, q=QB, h=2)
        blocked = cache[:, CACHED - 1]
        sq_x = cache[:, 0, :, :].rearrange("p j r -> p (j r)")[:, 0:T * D].rearrange("p (t d) -> p t d", d=D)

        v_sum = [bank(f"v_sum{b}") for b in range(XB)]
        flip = [bank(f"flip{b}") for b in range(2)]
        prep = bank("prep")
        h_sum = [f[:, 0:P] for f in flip]
        centered = [v_sum[b][:, 0:D] for b in range(2)]

        x_in = sem("x_in")
        params_in = sem("params_in")
        diag_zero = sem("diag_zero")
        diag_in = sem("diag_in")
        consts = sem("consts")
        pool_step = sem("pool_step")
        dve_step = sem("dve_step")
        x_centered = sem("x_centered")
        x_squared = sem("x_squared")
        x_var = sem("x_var")
        x_std = sem("x_std")
        res_ready = sem("res_ready")
        xr_ready = sem("xr_ready")
        w_ready = sem("w_ready")
        tile_in = [sem(f"tile_in{s}") for s in range(SLOTS)]
        tile_used = sem("tile_used")
        scaled_ready = sem("scaled_ready")
        prep_ready = sem("prep_ready")
        scaled_t_ready = sem("scaled_t_ready")
        e_ready = sem("e_ready")
        flipped = sem("flipped")
        cached_act = sem("cached_act")
        cached_dve = sem("cached_dve")
        v_summed = sem("v_summed")
        vt_act = sem("vt_act")
        vt_dve = sem("vt_dve")
        blocked_act = sem("blocked_act")
        blocked_dve = sem("blocked_dve")
        v_flipped = sem("v_flipped")
        v_act = sem("v_act")
        v_dve = sem("v_dve")
        index_step = sem("index_step")
        index_ready = sem("index_ready")
        gathers_due = sem("gathers_due")
        run_in = [[sem(f"run_in{b}{a}") for a in range(A)] for b in range(2)]
        run_turned = sem("run_turned")
        h_summed = sem("h_summed")
        h_t_ready = sem("h_t_ready")
        h_centered = sem("h_centered")
        h_squared = sem("h_squared")
        std_ready = sem("std_ready")
        fin_step = sem("fin_step")
        y_ready = sem("y_ready")
        stored = sem("stored")

        adj_tiles = adj.rearrange("(p t) c -> t p c", t=T)
        adj_runs = adj.rearrange("r (g c) -> (r g) c", g=G)
        out_rows = out.rearrange("(p t) d -> p t d", t=T)

        def at_least(eng, s, count):
            if not isinstance(count, int) or count > 0:
                eng.wait_ge(s, count)

        def tile_of(i, k):
            if k >= ITER:
                i, k = i + 1, k - ITER
            if k == CACHE_AT:
                return i + STREAMED
            return i * (ITER - 1) + (k if k < CACHE_AT else k - 1)

        def iterations(eng, body):
            body(0)
            with eng.Fori(1, CACHED - 1) as i:
                body(i)
            body(CACHED - 1)

        def copy_to_blocks(eng, copy, i, first, done):
            n = i * ITER + CACHE_AT
            slot = CACHE_AT % SLOTS
            at_least(eng, tile_used, n - ITER + 1)
            eng.wait_ge(tile_in[slot], (i * (ITER // SLOTS) + (CACHE_AT // SLOTS + 1)) * 16)
            for g in range(first, G, 2):
                last = copy(blocked[:, :, SQ * g:SQ * g + SQ],
                            work[:, slot, RUN * g:RUN * g + RUN].rearrange("p (j c) -> p j c", c=SQ))
            last.then_inc(done, 1)

        block = ctx.enter_context(nc.Block())

        @block.sync
        def _(sp):
            sp.dma_start(xr[:], x.rearrange("(p t) d -> p t d", t=T)).then_inc(x_in, 16)
            sp.dma_start(w_both[0:D, :], W_u).then_inc(params_in, 16)
            sp.dma_start(w_both[D:P, :], W_i).then_inc(params_in, 16)
            sp.dma_start(par[0:D, :], par_u.rearrange("(a n) -> a n", a=1).to_broadcast([D, 2])).then_inc(params_in, 16)
            sp.dma_start(par[D:P, :], par_i.rearrange("(a n) -> a n", a=1).to_broadcast([D, 2])).then_inc(params_in, 16)
            sp.dma_start(gamma[:], ln_gamma.rearrange("(a n) -> a n", a=1).to_broadcast([P, D])).then_inc(params_in, 16)
            sp.dma_start(beta[:], ln_beta.rearrange("(a n) -> a n", a=1).to_broadcast([P, D])).then_inc(params_in, 16)

            full, rest = NU // T, NU % T
            sp.wait_ge(diag_zero, 1)
            sp.dma_start(diag[0:full, 0, :], diag_u[0:full * T].rearrange("(p t) -> p t", t=T)).then_inc(diag_in, 16)
            sp.dma_start(diag[full:full + 1, 0, 0:rest],
                         diag_u[full * T:NU].rearrange("(p t) -> p t", p=1)).then_inc(diag_in, 16)
            sp.dma_start(diag[full:full + 1, 1, rest:T],
                         diag_i[0:T - rest].rearrange("(p t) -> p t", p=1)).then_inc(diag_in, 16)
            sp.dma_start(diag[full + 1:P, 1, :],
                         diag_i[T - rest:N - NU].rearrange("(p t) -> p t", t=T)).then_inc(diag_in, 16)

            def load(i):
                for k in range(ITER):
                    n = i * ITER + k
                    at_least(sp, tile_used, n - SLOTS + 1)
                    sp.dma_start(work[:, k % SLOTS, :], adj_tiles[tile_of(i, k)]).then_inc(tile_in[k % SLOTS], 16)

            iterations(sp, load)

            stores = 0
            position = 0
            for step in PLAN:
                if step[0] == "cached":
                    position += 1
                    if step[1] == CACHED - 1:
                        sp.wait_ge(y_ready, position)
                        sp.dma_start(out_rows[:, STREAMED:T, :], xr[:, STREAMED:T, :]).then_inc(stored, 16)
                        stores += 1
                else:
                    tiles = 2 * step[2] if step[0] == "pairs" else 1
                    position += tiles
                    sp.wait_ge(y_ready, position)
                    sp.dma_start(out_rows[:, step[1]:step[1] + tiles, :],
                                 xr[:, step[1]:step[1] + tiles, :]).then_inc(stored, 16)
                    stores += 1
            sp.wait_ge(stored, 16 * stores)

        @block.gpsimd
        def _(pool):
            nc.gpsimd.memset(diag[:], 0.0).then_inc(diag_zero, 1)
            nc.gpsimd.memset(eps[:], EPS)
            nc.gpsimd.memset(ident[:], 0.0)
            nc.gpsimd.memset(center[:], -1.0 / D).then_inc(pool_step, 1)
            pool.wait_ge(pool_step, 1)
            nc.gpsimd.affine_select(out=ident[:], in_=ident[:], compare_op=ALU.not_equal, fill=1.0, base=0,
                                    pattern=[[-1, P]], channel_multiplier=1)
            nc.gpsimd.affine_select(out=center[:], in_=center[:], compare_op=ALU.not_equal, fill=1.0 - 1.0 / D,
                                    base=0, pattern=[[-1, D]], channel_multiplier=1).then_inc(pool_step, 1)
            pool.wait_ge(pool_step, 2)
            nc.gpsimd.affine_select(out=center[:], in_=center[:], compare_op=ALU.not_equal, fill=1.0 - 1.0 / D,
                                    base=-D, pattern=[[-1, D]], channel_multiplier=1).then_inc(consts, 1)
            pool.wait_ge(consts, 1)
            for g in range(G):
                nc.gpsimd.iota(run_at[SQ * g:SQ * g + SQ], pattern=[[G, 2], [SQ * T * G, A]], base=g,
                               channel_multiplier=T * G).then_inc(index_step, 1)
                pool.wait_ge(index_step, g + 1)
            nc.gpsimd.iota(two_tiles[:], pattern=[[0, A]], base=2 * G, channel_multiplier=0).then_inc(index_ready, 1)

            pool.wait_ge(params_in, 6 * 16)
            beta_all = beta[:].rearrange("p (a d) -> p a d", a=1).to_broadcast([P, ITER, D])
            for c in range(CACHED):
                chunk = xr[:, ITER * c:ITER * c + ITER, :]
                pool.wait_ge(res_ready, c + 1)
                nc.gpsimd.tensor_tensor(chunk, chunk, hv[:, ITER * c:ITER * c + ITER, :], ALU.add).then_inc(pool_step, 1)
                pool.wait_ge(pool_step, 3 + c)
                nc.gpsimd.tensor_tensor(chunk, chunk, beta_all, ALU.add).then_inc(xr_ready, 1)

            def gather(b):
                for a in range(A):
                    nc.gpsimd.indirect_dma_start(
                        out=gathered[:, b, a, :], out_offset=None, in_=adj_runs,
                        in_offset=bass.IndirectOffsetOnAxis(ap=run_at[:, b, a:a + 1], axis=0),
                    ).then_inc(run_in[b][a], 16)

            pool.wait_ge(index_ready, 1)
            pool.wait_ge(tile_used, T - 1)
            gather(0)
            pool.wait_ge(v_summed, XB)
            gather(1)

            def gather_next(m, b):
                pool.wait_ge(run_turned, A * (m - 1))
                nc.gpsimd.tensor_tensor(run_at[:, b, :], run_at[:, b, :], two_tiles[:], ALU.add).then_inc(index_ready, 1)
                pool.wait_ge(index_ready, m)
                pool.sem_inc(gathers_due, 1)
                gather(b)

            with pool.Fori(1, STREAMED // 2) as i:
                gather_next(i * 2, 0)
                gather_next(i * 2 + 1, 1)
            gather_next(STREAMED - 1, 0)

        @block.scalar
        def _(act):
            act.wait_ge(consts, 1)
            for c in range(CACHED):
                part = slice(ITER * c, ITER * c + ITER)
                act.wait_ge(x_centered, c + 1)
                nc.scalar.activation(sq_x[:, part, :], hv[:, part, :], ACT.Square).then_inc(x_squared, 1)
                act.wait_ge(x_var, c + 1)
                nc.scalar.activation(stat[:, 1, part], stat[:, 0, part], ACT.Sqrt, bias=eps[:],
                                     scale=1.0 / D).then_inc(x_std, 1)

            def keep_blocks(i):
                copy_to_blocks(act, nc.scalar.copy, i, 0, blocked_act)
                for c in range(0, CG, 2):
                    act.wait_ge(flipped, i * (CG - 1) + c + 1)
                    nc.scalar.copy(cache[:, i, 4 * c:4 * c + 4, :].rearrange("p j r -> p (j r)"),
                                   flip[0][:]).then_inc(cached_act, 1)

            iterations(act, keep_blocks)

            for b in range(0, XB, 2):
                act.wait_ge(v_summed, b + 1)
                if b == 0:
                    act.wait_ge(tile_used, T - 2)
                nc.scalar.copy(vt[:, b].rearrange("p q g c -> p g q c"),
                               v_sum[b][:].rearrange("p (g q c) -> p g q c", g=G, q=QB)).then_inc(vt_act, 1)
            act.wait_ge(xr_ready, CACHED)
            for b in range(0, XB, 2):
                act.wait_ge(v_flipped, b + 1)
                nc.scalar.copy(v[:, b].rearrange("p q h d -> p (q h d)"), flip[b % 2][:]).then_inc(v_act, 1)

            def spread(s, odd):
                act.wait_ge(h_centered, s + 1)
                at_least(act, y_ready, s - 1)
                nc.scalar.activation(square[:], centered[odd], ACT.Square,
                                     accum_out=ssq[:, odd:odd + 1]).then_inc(h_squared, 1)
                act.wait_ge(h_squared, s + 1)
                nc.scalar.activation(std[:, odd:odd + 1], ssq[:, odd:odd + 1], ACT.Sqrt, bias=eps[:],
                                     scale=1.0 / D).then_inc(std_ready, 1)

            def take_sum(s, odd):
                act.wait_ge(h_summed, s + 1)
                at_least(act, h_centered, s - 1)
                nc.scalar.copy(h_t[:, odd, :], h_sum[odd]).then_inc(h_t_ready, 1)

            take_sum(0, 0)
            spread(0, 0)
            take_sum(1, 1)
            with act.Fori(1, T // 2) as i:
                spread(i * 2 - 1, 1)
                take_sum(i * 2, 0)
                spread(i * 2, 0)
                take_sum(i * 2 + 1, 1)
            spread(T - 1, 1)

        @block.vector
        def _(dve):
            dve.wait_ge(x_in, 16)
            steps = 0
            for c in range(CACHED):
                part = slice(ITER * c, ITER * c + ITER)

                def spread_out(s):
                    return stat[:, s, part].rearrange("p (t a) -> p t a", a=1).to_broadcast([P, ITER, D])

                nc.vector.tensor_reduce(stat[:, 0, part], xr[:, part, :], AX_X, ALU.add).then_inc(dve_step, 1)
                dve.wait_ge(dve_step, steps + 1)
                nc.vector.tensor_scalar(stat[:, 0, part], stat[:, 0, part], 1.0 / D, None, ALU.mult).then_inc(dve_step, 1)
                dve.wait_ge(dve_step, steps + 2)
                nc.vector.tensor_tensor(hv[:, part, :], xr[:, part, :], spread_out(0), ALU.subtract).then_inc(x_centered, 1)
                dve.wait_ge(x_squared, c + 1)
                nc.vector.tensor_reduce(stat[:, 0, part], sq_x[:, part, :], AX_X, ALU.add).then_inc(x_var, 1)
                dve.wait_ge(x_std, c + 1)
                nc.vector.reciprocal(stat[:, 2, part], stat[:, 1, part]).then_inc(dve_step, 1)
                dve.wait_ge(dve_step, steps + 3)
                nc.vector.scalar_tensor_tensor(out=hv[:, part, :], in0=hv[:, part, :], scalar=0.0, in1=spread_out(2),
                                               op0=ALU.max, op1=ALU.mult).then_inc(res_ready, 1)
                steps += 3
            dve.wait_ge(params_in, 6 * 16)
            nc.vector.tensor_scalar(w_both[:], w_both[:], par[:, 0:1], par[:, 1:2], ALU.mult, ALU.mult).then_inc(w_ready, 1)
            dve.wait_ge(diag_in, 4 * 16)
            dve.wait_ge(res_ready, CACHED)

            def scale(t, n, odd):
                at_least(dve, prep_ready, n - 1)
                nc.vector.tensor_scalar(scaled[:, odd, 0, :], hv[:, t, :], diag[:, 0, bass.ds(t, 1)], None, ALU.mult)
                nc.vector.tensor_scalar(scaled[:, odd, 1, :], hv[:, t, :], diag[:, 1, bass.ds(t, 1)], None,
                                        ALU.mult).then_inc(scaled_ready, 1)

            def take_e(t, n, odd):
                dve.wait_ge(prep_ready, n + 2)
                at_least(dve, tile_used, n - 1)
                nc.vector.tensor_tensor(e_tile[:, odd, :], prep[:, P:P + D], hv[:, t, :], ALU.add).then_inc(e_ready, 1)

            def take_scaled_t(n, odd):
                dve.wait_ge(prep_ready, n + 1)
                nc.vector.tensor_copy(scaled_t[:, odd, :], prep[:, 0:P]).then_inc(scaled_t_ready, 1)

            scale(0, 0, 0)
            scale(1, 1, 1)
            take_scaled_t(0, 0)
            take_e(0, 0, 0)
            take_scaled_t(1, 1)

            def prepare(i):
                for k in range(ITER):
                    n = i * ITER + k
                    static = isinstance(n, int)
                    if not static or n + 2 < T:
                        scale(tile_of(i, k + 2), n + 2, k % 2)
                    if not static or n + 1 < T:
                        take_e(tile_of(i, k + 1), n + 1, (k + 1) % 2)
                    if not static or n + 2 < T:
                        take_scaled_t(n + 2, k % 2)
                    if k == CACHE_AT:
                        copy_to_blocks(dve, nc.vector.tensor_copy, i, 1, blocked_dve)
                        for c in range(1, CG, 2):
                            if c < CG - 1:
                                dve.wait_ge(flipped, i * (CG - 1) + c + 1)
                            else:
                                dve.wait_ge(tile_used, n + 1)
                            nc.vector.tensor_copy(cache[:, i, 4 * c:4 * c + 4, :].rearrange("p j r -> p (j r)"),
                                                  flip[1][:]).then_inc(cached_dve, 1)

            iterations(dve, prepare)

            for b in range(1, XB, 2):
                dve.wait_ge(v_summed, b + 1)
                if b == 1:
                    dve.wait_ge(tile_used, T - 2)
                nc.vector.tensor_copy(vt[:, b].rearrange("p q g c -> p g q c"),
                                      v_sum[b][:].rearrange("p (g q c) -> p g q c", g=G, q=QB)).then_inc(vt_dve, 1)
            dve.wait_ge(xr_ready, CACHED)
            for b in range(1, XB, 2):
                dve.wait_ge(v_flipped, b + 1)
                nc.vector.tensor_copy(v[:, b].rearrange("p q h d -> p (q h d)"), flip[b % 2][:]).then_inc(v_dve, 1)

            def finish(s, odd, t):
                dve.wait_ge(std_ready, s + 1)
                nc.vector.reciprocal(rstd[:, odd:odd + 1], std[:, odd:odd + 1]).then_inc(fin_step, 1)
                yield
                dve.wait_ge(fin_step, s * 2 + 1)
                nc.vector.scalar_tensor_tensor(out=z[:, odd, :], in0=centered[odd], scalar=rstd[:, odd:odd + 1],
                                               in1=gamma[:], op0=ALU.mult, op1=ALU.mult).then_inc(fin_step, 1)
                yield
                dve.wait_ge(fin_step, s * 2 + 2)
                nc.vector.tensor_tensor(xr[:, t, :], xr[:, t, :], z[:, odd, :], ALU.add).then_inc(y_ready, 1)
                yield

            def turn(b, count, used, finishing):
                if isinstance(count, int) and count == 1 and b == 1:
                    dve.wait_ge(v_flipped, XB)
                at_least(dve, h_summed, used)
                for a in range(A):
                    dve.wait_ge(run_in[b][a], count * 16)
                    nc.vector.transpose(turned[:, b, :, SQ * a:SQ * a + SQ],
                                        gathered[:, b, a, :].rearrange("p (j c) -> p j c", c=SQ)).then_inc(run_turned, 1)
                    next(finishing, None)

            def two_back(s):
                return finish(s - 2, (s - 2) % 2, ORDER[s - 2]) if s >= 2 else iter(())

            def summed_with(m):
                return ORDER.index(m) + 1 if m >= 0 else 0

            position = 0
            for step in PLAN:
                if step[0] == "cached":
                    for _ in two_back(position):
                        pass
                    position += 1
                elif step[0] == "single":
                    turn(step[1] % 2, step[1] // 2 + 1, summed_with(step[1] - 2), two_back(position))
                    position += 1
                else:
                    _, m0, pairs = step
                    for k in range(2):
                        turn(k, m0 // 2 + 1, summed_with(m0 + k - 2), two_back(position + k))
                    s0 = position
                    with dve.Fori(1, pairs) as i:
                        for k in range(2):
                            turn(k, i + (m0 // 2 + 1), i * 2 + (s0 + k - 1),
                                 finish(i * 2 + (s0 + k - 2), (s0 + k) % 2, i * 2 + (m0 + k - 2)))
                    position += 2 * pairs
            for s in (T - 2, T - 1):
                for _ in finish(s, s % 2, ORDER[s]):
                    pass

        @block.tensor
        def _(pe):
            pe.wait_ge(consts, 1)

            def product(n, odd):
                pe.wait_ge(scaled_t_ready, n + 1)
                at_least(pe, e_ready, n)
                return nc.tensor.matmul(prep[:, P:P + D], scaled_t[:, odd, :], w_both[:], start=True, stop=True)

            def flip_scaled(n, odd):
                pe.wait_ge(scaled_ready, n + 1)
                at_least(pe, scaled_t_ready, n)
                return nc.tensor.transpose(prep[:, 0:P], scaled[:, odd].rearrange("p h d -> p (h d)"), ident[:])

            flip_scaled(0, 0).then_inc(prep_ready, 1)
            pe.wait_ge(w_ready, 1)
            product(0, 0)
            flip_scaled(1, 1).then_inc(prep_ready, 1)

            def add_tiles(i):
                for k in range(ITER):
                    n = i * ITER + k
                    static = isinstance(n, int)
                    slot = k % SLOTS
                    columns = work[:, slot, :].rearrange("p (g h c) -> p g h c", g=G, h=2)
                    pe.wait_ge(tile_in[slot], (i * (ITER // SLOTS) + (k // SLOTS + 1)) * 16)
                    pe.wait_ge(e_ready, n + 1)
                    for b in range(XB):
                        for h in range(2):
                            last = nc.tensor.matmul(v_sum[b][D * h:D * h + D, :].rearrange("d (g c) -> d g c", g=G),
                                                    e_tile[:, k % 2, :], columns[:, :, h, P * b:P * b + P],
                                                    start=static and n == 0, stop=static and n == T - 1)
                        if static and n == T - 1:
                            last.then_inc(v_summed, 1)
                        if b == 2 and not (static and n + 1 >= T):
                            ready = product(n + 1, (k + 1) % 2)
                            if not static or n + 2 < T:
                                ready = flip_scaled(n + 2, k % 2)
                            ready.then_inc(prep_ready, 1)
                    if k == CACHE_AT:
                        pe.wait_ge(blocked_act, i + 1)
                        pe.wait_ge(blocked_dve, i + 1)
                        for c in range(CG):
                            at_least(pe, cached_dve if c % 2 else cached_act, i * (CG // 2) + c // 2)
                            for q in range(4):
                                last = nc.tensor.transpose(flip[c % 2][:, P * q:P * q + P], blocked[:, 4 * c + q, :],
                                                           ident[:])
                            if c < CG - 1:
                                last.then_inc(flipped, 1)
                    if not (static and n == T - 1):
                        last.then_inc(tile_used, 1)

            iterations(pe, add_tiles)

            for b in range(XB):
                if b % 2:
                    pe.wait_ge(vt_dve, b // 2 + 1)
                    at_least(pe, v_dve, b // 2)
                else:
                    pe.wait_ge(vt_act, b // 2 + 1)
                    at_least(pe, v_act, b // 2)
                for q in range(QB):
                    last = nc.tensor.transpose(flip[b % 2][:, P * q:P * q + P], vt[:, b, q].rearrange("p g c -> p (g c)"),
                                               ident[:])
                last.then_inc(v_flipped, 1)
            pe.wait_ge(v_act, (XB + 1) // 2)
            pe.wait_ge(v_dve, XB // 2)

            def center_rows(s, odd):
                pe.wait_ge(h_t_ready, s + 1)
                at_least(pe, y_ready, s - 1)
                nc.tensor.matmul(centered[odd], h_t[:, odd, :], center[:], start=True, stop=True).then_inc(h_centered, 1)

            def add_blocks(s, odd, rows):
                at_least(pe, h_t_ready, s - 1)
                for j in range(J // 2):
                    for h in range(2):
                        last = nc.tensor.matmul(h_sum[odd][D * h:D * h + D, :], v[:, j // QB, j % QB, h, :],
                                                rows[:, h * (J // 2) + j, :], start=j == 0, stop=j == J // 2 - 1)
                    if j == J // 4 and not (isinstance(s, int) and s == 0):
                        center_rows(s - 1, 1 - odd)
                last.then_inc(h_summed, 1)

            def add_streamed(s, odd, m, b):
                pe.wait_ge(run_turned, (m + 1) * A)
                add_blocks(s, odd, turned[:, b])

            position = 0
            for step in PLAN:
                if step[0] == "cached":
                    pe.wait_ge(cached_act, CACHED * CG // 2)
                    pe.wait_ge(cached_dve, CACHED * CG // 2)
                    add_blocks(position, position % 2, cache[:, step[1]])
                    position += 1
                elif step[0] == "single":
                    add_streamed(position, position % 2, step[1], step[1] % 2)
                    position += 1
                else:
                    _, m0, pairs = step
                    s0 = position
                    with pe.Fori(0, pairs) as i:
                        for k in range(2):
                            add_streamed(i * 2 + (s0 + k), (s0 + k) % 2, i * 2 + (m0 + k), k)
                    position += 2 * pairs
            center_rows(T - 1, 1)


INPUTS = ['x', 'adj', 'L0_gnn_W_u', 'L0_gnn_diag_u', 'L0_gnn_par_u', 'L0_gnn_W_i', 'L0_gnn_diag_i', 'L0_gnn_par_i',
          'L0_gnn_ln_gamma', 'L0_gnn_ln_beta']


def kernel(**inputs):
    import numpy as np
    import concourse.bacc as bacc
    from concourse.bass_utils import run_bass_kernel_spmd

    nc = bacc.Bacc("TRN2", target_bir_lowering=False, num_devices=1)
    arrays, args = {}, []
    for name in INPUTS:
        a = np.ascontiguousarray(inputs[name])
        arrays[name + "_dram"] = a
        args.append(nc.dram_tensor(name + "_dram", a.shape, mybir.dt.from_np(a.dtype), kind="ExternalInput").ap())
    out = nc.dram_tensor("out_dram", inputs['x'].shape, F32, kind="ExternalOutput").ap()
    build(nc, *args, out)
    return run_bass_kernel_spmd(nc, [arrays], core_ids=[0]).results[0]["out_dram"]
```

```python
from contextlib import ExitStack

import concourse.bass as bass
from concourse import mybir

F32 = mybir.dt.float32
U32 = mybir.dt.uint32
ALU = mybir.AluOpType
ACT = mybir.ActivationFunctionType
AX_X = mybir.AxisListType.X

P = 128
EPS = 1e-5

G = 4
SQ = 32


def build(nc, x, adj, W_u, diag_u, par_u, W_i, diag_i, par_i, ln_gamma, ln_beta, out):
    N, D = x.shape
    T = N // P
    NU = diag_u.shape[0]
    RUN = N // G
    HALF = RUN // 2
    XB = HALF // P
    QB = P // SQ
    J = RUN // SQ
    A = P // SQ
    assert G * RUN == N and XB * P == HALF and 2 * D == P and XB == 5

    CACHED = 5
    STREAMED = T - CACHED
    ITER = T // CACHED
    CACHE_AT = 3
    SLOTS = 4
    assert ITER * CACHED == T and ITER % SLOTS == 0
    CENTER_AFTER = 3
    CG = J // 4

    X_ORDER = [0, CACHED - 1, *range(1, CACHED - 1)]

    PLAN = [("cached", 0), ("cached", 1), ("pairs", 0, 6), ("cached", 2), ("cached", 3), ("pairs", 12, 6),
            ("cached", 4), ("pairs", 24, 5), ("single", STREAMED - 1)]
    ORDER = []
    for step in PLAN:
        if step[0] == "cached":
            ORDER.append(STREAMED + step[1])
        elif step[0] == "single":
            ORDER.append(step[1])
        else:
            ORDER += range(step[1], step[1] + 2 * step[2])
    assert sorted(ORDER) == list(range(T))

    with ExitStack() as ctx:
        def sb(name, shape, dt=F32):
            return ctx.enter_context(nc.sbuf_tensor(name, shape, dt))

        def bank(name):
            return ctx.enter_context(nc.psum_tensor(name, [P, 512], F32))

        def sem(name):
            return ctx.enter_context(nc.semaphore(name))

        work = sb("work", [P, SLOTS, N])
        cache = sb("cache", [P, CACHED, J, P])
        hv = sb("hv", [P, T, D])
        xr = sb("xr", [P, T, D])
        ident = sb("ident", [P, P])
        center = sb("center", [P, D])
        w_both = sb("w_both", [P, D])
        par = sb("par", [P, 2])
        diag = sb("diag", [P, 2, T])
        gamma = sb("gamma", [P, D])
        beta = sb("beta", [P, D])
        scaled = sb("scaled", [P, 2, 2, D])
        scaled_t = sb("scaled_t", [P, 2, P])
        e_tile = sb("e_tile", [P, 2, D])
        stat = sb("stat", [P, 3, T])
        square = sb("square", [P, D])
        h_t = sb("h_t", [P, 2, P])
        ssq = sb("ssq", [P, 2])
        std = sb("std", [P, 2])
        rstd = sb("rstd", [P, 2])
        z = sb("z", [P, 2, D])
        eps = sb("eps", [P, 1])
        two_tiles = sb("two_tiles", [P, A], U32)
        run_at = sb("run_at", [P, 2, A], U32)

        turned = work[:, 0:2, :].rearrange("p b (j r) -> p b j r", r=P)
        gathered = work[:, 2:4, :].rearrange("p b (a c) -> p b a c", a=A)
        vt = work[:, 1, 0:XB * 512].rearrange("p (b q g c) -> p b q g c", b=XB, q=QB, g=G)
        v = hv[:].rearrange("p t d -> p (t d)").rearrange("p (b q h d) -> p b q h d", b=XB, q=QB, h=2)
        blocked = cache[:, CACHED - 1]
        sq_x = cache[:, 0, :, :].rearrange("p j r -> p (j r)")[:, 0:T * D].rearrange("p (t d) -> p t d", d=D)

        v_sum = [bank(f"v_sum{b}") for b in range(XB)]
        flip = [bank(f"flip{b}") for b in range(2)]
        prep = bank("prep")
        h_sum = [f[:, 0:P] for f in flip]
        centered = [v_sum[b][:, 0:D] for b in range(2)]

        x_in = [sem(f"x_in{c}") for c in range(CACHED)]
        w_in = sem("w_in")
        diag_zero = sem("diag_zero")
        norm_in = sem("norm_in")
        diag_in = sem("diag_in")
        eps_ready = sem("eps_ready")
        consts = sem("consts")
        pool_step = sem("pool_step")
        dve_step = sem("dve_step")
        x_centered = sem("x_centered")
        x_squared = sem("x_squared")
        x_var = sem("x_var")
        x_std = sem("x_std")
        res_ready = sem("res_ready")
        xr_ready = sem("xr_ready")
        w_ready = sem("w_ready")
        tile_in = [sem(f"tile_in{s}") for s in range(SLOTS)]
        tile_used = sem("tile_used")
        scaled_ready = sem("scaled_ready")
        prep_ready = sem("prep_ready")
        scaled_t_ready = sem("scaled_t_ready")
        e_ready = sem("e_ready")
        flipped = sem("flipped")
        cached_act = sem("cached_act")
        cached_dve = sem("cached_dve")
        v_summed = sem("v_summed")
        vt_act = sem("vt_act")
        vt_dve = sem("vt_dve")
        blocked_act = sem("blocked_act")
        blocked_dve = sem("blocked_dve")
        v_flipped = sem("v_flipped")
        v_act = sem("v_act")
        v_dve = sem("v_dve")
        index_step = sem("index_step")
        index_ready = sem("index_ready")
        gathers_due = sem("gathers_due")
        run_in = [[sem(f"run_in{b}{a}") for a in range(A)] for b in range(2)]
        run_turned = sem("run_turned")
        h_summed = sem("h_summed")
        h_t_ready = sem("h_t_ready")
        h_centered = sem("h_centered")
        h_squared = sem("h_squared")
        std_ready = sem("std_ready")
        fin_step = sem("fin_step")
        y_ready = sem("y_ready")
        stored = sem("stored")

        adj_tiles = adj.rearrange("(p t) c -> t p c", t=T)
        adj_runs = adj.rearrange("r (g c) -> (r g) c", g=G)
        x_rows = x.rearrange("(p t) d -> p t d", t=T)
        out_rows = out.rearrange("(p t) d -> p t d", t=T)

        def at_least(eng, s, count):
            if not isinstance(count, int) or count > 0:
                eng.wait_ge(s, count)

        def tile_of(i, k):
            if k >= ITER:
                i, k = i + 1, k - ITER
            if k == CACHE_AT:
                return i + STREAMED
            return i * (ITER - 1) + (k if k < CACHE_AT else k - 1)

        def iterations(eng, body):
            body(0)
            with eng.Fori(1, CACHED - 1) as i:
                body(i)
            body(CACHED - 1)

        def copy_to_blocks(eng, copy, i, first, done):
            n = i * ITER + CACHE_AT
            slot = CACHE_AT % SLOTS
            at_least(eng, tile_used, n - ITER + 1)
            eng.wait_ge(tile_in[slot], (i * (ITER // SLOTS) + (CACHE_AT // SLOTS + 1)) * 16)
            for g in range(first, G, 2):
                last = copy(blocked[:, :, SQ * g:SQ * g + SQ],
                            work[:, slot, RUN * g:RUN * g + RUN].rearrange("p (j c) -> p j c", c=SQ))
            last.then_inc(done, 1)

        def row_of(vector):
            return vector.rearrange("(a n) -> a n", a=1)

        def part_of(c):
            return slice(ITER * c, ITER * c + ITER)

        def load_x(eng, c):
            eng.dma_start(xr[:, part_of(c), :], x_rows[:, part_of(c), :]).then_inc(x_in[c], 16)

        block = ctx.enter_context(nc.Block())

        @block.sync
        def _(sp):
            load_x(sp, X_ORDER[0])
            load_x(sp, X_ORDER[1])
            sp.dma_start(w_both[0:D, :], W_u).then_inc(w_in, 16)
            sp.dma_start(w_both[D:P, :], W_i).then_inc(w_in, 16)
            def load(i):
                for k in range(ITER):
                    n = i * ITER + k
                    at_least(sp, tile_used, n - SLOTS + 1)
                    sp.dma_start(work[:, k % SLOTS, :], adj_tiles[tile_of(i, k)]).then_inc(tile_in[k % SLOTS], 16)
                    if isinstance(n, int) and n == 0:
                        for c in X_ORDER[2:]:
                            load_x(sp, c)
                    if isinstance(n, int) and n == 1:
                        sp.dma_start(gamma[:], row_of(ln_gamma).to_broadcast([P, D])).then_inc(norm_in, 16)
                        sp.dma_start(beta[:], row_of(ln_beta).to_broadcast([P, D])).then_inc(norm_in, 16)

            iterations(sp, load)

            stores = 0
            position = 0
            for step in PLAN:
                if step[0] == "cached":
                    position += 1
                    if step[1] == CACHED - 1:
                        sp.wait_ge(y_ready, position)
                        sp.dma_start(out_rows[:, STREAMED:T, :], xr[:, STREAMED:T, :]).then_inc(stored, 16)
                        stores += 1
                else:
                    tiles = 2 * step[2] if step[0] == "pairs" else 1
                    position += tiles
                    sp.wait_ge(y_ready, position)
                    sp.dma_start(out_rows[:, step[1]:step[1] + tiles, :],
                                 xr[:, step[1]:step[1] + tiles, :]).then_inc(stored, 16)
                    stores += 1
            sp.wait_ge(stored, 16 * stores)

        @block.gpsimd
        def _(pool):
            nc.gpsimd.memset(diag[:], 0.0).then_inc(diag_zero, 1)
            nc.gpsimd.memset(eps[:], EPS).then_inc(eps_ready, 1)
            nc.gpsimd.memset(ident[:], 0.0)
            nc.gpsimd.memset(center[:], -1.0 / D).then_inc(pool_step, 1)
            pool.wait_ge(pool_step, 1)
            nc.gpsimd.affine_select(out=ident[:], in_=ident[:], compare_op=ALU.not_equal, fill=1.0, base=0,
                                    pattern=[[-1, P]], channel_multiplier=1)
            nc.gpsimd.affine_select(out=center[:], in_=center[:], compare_op=ALU.not_equal, fill=1.0 - 1.0 / D,
                                    base=0, pattern=[[-1, D]], channel_multiplier=1).then_inc(pool_step, 1)
            pool.wait_ge(pool_step, 2)
            nc.gpsimd.affine_select(out=center[:], in_=center[:], compare_op=ALU.not_equal, fill=1.0 - 1.0 / D,
                                    base=-D, pattern=[[-1, D]], channel_multiplier=1).then_inc(consts, 1)
            pool.wait_ge(consts, 1)
            for g in range(G):
                nc.gpsimd.iota(run_at[SQ * g:SQ * g + SQ], pattern=[[G, 2], [SQ * T * G, A]], base=g,
                               channel_multiplier=T * G).then_inc(index_step, 1)
                pool.wait_ge(index_step, g + 1)
            nc.gpsimd.iota(two_tiles[:], pattern=[[0, A]], base=2 * G, channel_multiplier=0).then_inc(index_ready, 1)

            pool.wait_ge(norm_in, 2 * 16)
            beta_all = beta[:].rearrange("p (a d) -> p a d", a=1).to_broadcast([P, ITER, D])
            for count, c in enumerate(X_ORDER):
                chunk = xr[:, part_of(c), :]
                pool.wait_ge(res_ready, count + 1)
                nc.gpsimd.tensor_tensor(chunk, chunk, hv[:, part_of(c), :], ALU.add).then_inc(pool_step, 1)
                pool.wait_ge(pool_step, 3 + count)
                nc.gpsimd.tensor_tensor(chunk, chunk, beta_all, ALU.add).then_inc(xr_ready, 1)

            def gather(b):
                for a in range(A):
                    nc.gpsimd.indirect_dma_start(
                        out=gathered[:, b, a, :], out_offset=None, in_=adj_runs,
                        in_offset=bass.IndirectOffsetOnAxis(ap=run_at[:, b, a:a + 1], axis=0),
                    ).then_inc(run_in[b][a], 16)

            pool.wait_ge(index_ready, 1)
            pool.wait_ge(tile_used, T - 1)
            gather(0)
            pool.wait_ge(v_summed, XB)
            gather(1)

            def gather_next(m, b):
                pool.wait_ge(run_turned, A * (m - 1))
                nc.gpsimd.tensor_tensor(run_at[:, b, :], run_at[:, b, :], two_tiles[:], ALU.add).then_inc(index_ready, 1)
                pool.wait_ge(index_ready, m)
                pool.sem_inc(gathers_due, 1)
                gather(b)

            with pool.Fori(1, STREAMED // 2) as i:
                gather_next(i * 2, 0)
                gather_next(i * 2 + 1, 1)
            gather_next(STREAMED - 1, 0)

        @block.scalar
        def _(act):
            full, rest = NU // T, NU % T
            act.wait_ge(diag_zero, 1)
            act.dma_start(diag[0:full, 0, :], diag_u[0:full * T].rearrange("(p t) -> p t", t=T)).then_inc(diag_in, 16)
            act.dma_start(diag[full:full + 1, 0, 0:rest], row_of(diag_u[full * T:NU])).then_inc(diag_in, 16)
            act.dma_start(diag[full:full + 1, 1, rest:T], row_of(diag_i[0:T - rest])).then_inc(diag_in, 16)
            act.dma_start(diag[full + 1:P, 1, :],
                           diag_i[T - rest:N - NU].rearrange("(p t) -> p t", t=T)).then_inc(diag_in, 16)
            act.dma_start(par[0:D, :], row_of(par_u).to_broadcast([D, 2])).then_inc(w_in, 16)
            act.dma_start(par[D:P, :], row_of(par_i).to_broadcast([D, 2])).then_inc(w_in, 16)
            act.wait_ge(eps_ready, 1)
            nc.scalar.activation(std[:, 0:1], eps[:], ACT.Sqrt)
            for count, c in enumerate(X_ORDER):
                part = part_of(c)
                act.wait_ge(x_centered, count + 1)
                nc.scalar.activation(sq_x[:, part, :], hv[:, part, :], ACT.Square).then_inc(x_squared, 1)
                act.wait_ge(x_var, count + 1)
                nc.scalar.activation(stat[:, 1, part], stat[:, 0, part], ACT.Sqrt, bias=eps[:],
                                     scale=1.0 / D).then_inc(x_std, 1)

            def keep_blocks(i):
                copy_to_blocks(act, nc.scalar.copy, i, 0, blocked_act)
                for c in range(0, CG, 2):
                    act.wait_ge(flipped, i * (CG - 1) + c + 1)
                    nc.scalar.copy(cache[:, i, 4 * c:4 * c + 4, :].rearrange("p j r -> p (j r)"),
                                   flip[0][:]).then_inc(cached_act, 1)

            iterations(act, keep_blocks)

            for b in range(0, XB, 2):
                act.wait_ge(v_summed, b + 1)
                if b == 0:
                    act.wait_ge(tile_used, T - 2)
                nc.scalar.copy(vt[:, b].rearrange("p q g c -> p g q c"),
                               v_sum[b][:].rearrange("p (g q c) -> p g q c", g=G, q=QB)).then_inc(vt_act, 1)
            act.wait_ge(xr_ready, CACHED)
            for b in range(0, XB, 2):
                act.wait_ge(v_flipped, b + 1)
                nc.scalar.copy(v[:, b].rearrange("p q h d -> p (q h d)"), flip[b % 2][:]).then_inc(v_act, 1)

            def spread(s, odd):
                act.wait_ge(h_centered, s + 1)
                at_least(act, y_ready, s - 1)
                nc.scalar.activation(square[:], centered[odd], ACT.Square,
                                     accum_out=ssq[:, odd:odd + 1]).then_inc(h_squared, 1)
                act.wait_ge(h_squared, s + 1)
                nc.scalar.activation(std[:, odd:odd + 1], ssq[:, odd:odd + 1], ACT.Sqrt, bias=eps[:],
                                     scale=1.0 / D).then_inc(std_ready, 1)

            def take_sum(s, odd):
                act.wait_ge(h_summed, s + 1)
                at_least(act, h_centered, s - 1)
                nc.scalar.copy(h_t[:, odd, :], h_sum[odd]).then_inc(h_t_ready, 1)

            take_sum(0, 0)
            spread(0, 0)
            take_sum(1, 1)
            with act.Fori(1, T // 2) as i:
                spread(i * 2 - 1, 1)
                take_sum(i * 2, 0)
                spread(i * 2, 0)
                take_sum(i * 2 + 1, 1)
            spread(T - 1, 1)

        @block.vector
        def _(dve):
            def make_res(count):
                part = part_of(X_ORDER[count])

                def spread_out(s):
                    return stat[:, s, part].rearrange("p (t a) -> p t a", a=1).to_broadcast([P, ITER, D])

                dve.wait_ge(x_in[X_ORDER[count]], 16)
                nc.vector.tensor_reduce(stat[:, 0, part], xr[:, part, :], AX_X, ALU.add).then_inc(dve_step, 1)
                dve.wait_ge(dve_step, 3 * count + 1)
                nc.vector.tensor_scalar(stat[:, 0, part], stat[:, 0, part], 1.0 / D, None, ALU.mult).then_inc(dve_step, 1)
                dve.wait_ge(dve_step, 3 * count + 2)
                nc.vector.tensor_tensor(hv[:, part, :], xr[:, part, :], spread_out(0), ALU.subtract).then_inc(x_centered, 1)
                dve.wait_ge(x_squared, count + 1)
                nc.vector.tensor_reduce(stat[:, 0, part], sq_x[:, part, :], AX_X, ALU.add).then_inc(x_var, 1)
                dve.wait_ge(x_std, count + 1)
                nc.vector.reciprocal(stat[:, 2, part], stat[:, 1, part]).then_inc(dve_step, 1)
                dve.wait_ge(dve_step, 3 * count + 3)
                nc.vector.scalar_tensor_tensor(out=hv[:, part, :], in0=hv[:, part, :], scalar=0.0, in1=spread_out(2),
                                               op0=ALU.max, op1=ALU.mult).then_inc(res_ready, 1)

            make_res(0)
            dve.wait_ge(w_in, 4 * 16)
            nc.vector.tensor_scalar(w_both[:], w_both[:], par[:, 0:1], par[:, 1:2], ALU.mult, ALU.mult).then_inc(w_ready, 1)
            dve.wait_ge(diag_in, 4 * 16)
            dve.wait_ge(res_ready, 1)

            def scale(t, n, odd):
                at_least(dve, prep_ready, n - 1)
                nc.vector.tensor_scalar(scaled[:, odd, 0, :], hv[:, t, :], diag[:, 0, bass.ds(t, 1)], None, ALU.mult)
                nc.vector.tensor_scalar(scaled[:, odd, 1, :], hv[:, t, :], diag[:, 1, bass.ds(t, 1)], None,
                                        ALU.mult).then_inc(scaled_ready, 1)

            def take_e(t, n, odd):
                dve.wait_ge(prep_ready, n + 2)
                at_least(dve, tile_used, n - 1)
                nc.vector.tensor_tensor(e_tile[:, odd, :], prep[:, P:P + D], hv[:, t, :], ALU.add).then_inc(e_ready, 1)

            def take_scaled_t(n, odd):
                dve.wait_ge(prep_ready, n + 1)
                nc.vector.tensor_copy(scaled_t[:, odd, :], prep[:, 0:P]).then_inc(scaled_t_ready, 1)

            scale(0, 0, 0)
            scale(1, 1, 1)
            take_scaled_t(0, 0)
            take_e(0, 0, 0)
            take_scaled_t(1, 1)
            make_res(1)
            dve.wait_ge(res_ready, 2)

            def prepare(i):
                for k in range(ITER):
                    n = i * ITER + k
                    static = isinstance(n, int)
                    if not static or n + 2 < T:
                        scale(tile_of(i, k + 2), n + 2, k % 2)
                    if not static or n + 1 < T:
                        take_e(tile_of(i, k + 1), n + 1, (k + 1) % 2)
                    if not static or n + 2 < T:
                        take_scaled_t(n + 2, k % 2)
                    if static and n < CACHED - 2:
                        make_res(n + 2)
                        dve.wait_ge(res_ready, n + 3)
                    if k == CACHE_AT:
                        copy_to_blocks(dve, nc.vector.tensor_copy, i, 1, blocked_dve)
                        for c in range(1, CG, 2):
                            if c < CG - 1:
                                dve.wait_ge(flipped, i * (CG - 1) + c + 1)
                            else:
                                dve.wait_ge(tile_used, n + 1)
                            nc.vector.tensor_copy(cache[:, i, 4 * c:4 * c + 4, :].rearrange("p j r -> p (j r)"),
                                                  flip[1][:]).then_inc(cached_dve, 1)

            iterations(dve, prepare)

            for b in range(1, XB, 2):
                dve.wait_ge(v_summed, b + 1)
                if b == 1:
                    dve.wait_ge(tile_used, T - 2)
                nc.vector.tensor_copy(vt[:, b].rearrange("p q g c -> p g q c"),
                                      v_sum[b][:].rearrange("p (g q c) -> p g q c", g=G, q=QB)).then_inc(vt_dve, 1)
            dve.wait_ge(xr_ready, CACHED)
            for b in range(1, XB, 2):
                dve.wait_ge(v_flipped, b + 1)
                nc.vector.tensor_copy(v[:, b].rearrange("p q h d -> p (q h d)"), flip[b % 2][:]).then_inc(v_dve, 1)

            def finish(s, odd, t):
                dve.wait_ge(std_ready, s + 1)
                nc.vector.reciprocal(rstd[:, odd:odd + 1], std[:, odd:odd + 1]).then_inc(fin_step, 1)
                yield
                dve.wait_ge(fin_step, s * 2 + 1)
                nc.vector.scalar_tensor_tensor(out=z[:, odd, :], in0=centered[odd], scalar=rstd[:, odd:odd + 1],
                                               in1=gamma[:], op0=ALU.mult, op1=ALU.mult).then_inc(fin_step, 1)
                yield
                dve.wait_ge(fin_step, s * 2 + 2)
                nc.vector.tensor_tensor(xr[:, t, :], xr[:, t, :], z[:, odd, :], ALU.add).then_inc(y_ready, 1)
                yield

            def turn(b, count, used, finishing):
                if isinstance(count, int) and count == 1 and b == 1:
                    dve.wait_ge(v_flipped, XB)
                at_least(dve, h_summed, used)
                for a in range(A):
                    dve.wait_ge(run_in[b][a], count * 16)
                    nc.vector.transpose(turned[:, b, :, SQ * a:SQ * a + SQ],
                                        gathered[:, b, a, :].rearrange("p (j c) -> p j c", c=SQ)).then_inc(run_turned, 1)
                    if a > 0:
                        next(finishing, None)

            def summed_with(m):
                return ORDER.index(m) + 1 if m >= 0 else 0

            def finish_at(s):
                return finish(s, s % 2, ORDER[s])

            def finish_to(s, end):
                for p in range(s, end):
                    for _ in finish_at(p):
                        pass

            dve.wait_ge(norm_in, 2 * 16)
            position = 0
            finished = 0
            for step in PLAN:
                if step[0] == "cached":
                    position += 1
                elif step[0] == "single":
                    m = step[1]
                    turn(m % 2, m // 2 + 1, summed_with(m - 2), finish_at(finished))
                    finished += 1
                    position += 1
                else:
                    _, m0, pairs = step
                    for k in range(2):
                        late = m0 > 0
                        turn(k, m0 // 2 + 1, summed_with(m0 + k - 2), finish_at(finished) if late else iter(()))
                        finished += late
                    finish_to(finished, position)
                    s0 = position
                    with dve.Fori(1, pairs) as i:
                        for k in range(2):
                            turn(k, i + (m0 // 2 + 1), i * 2 + (s0 + k - 1),
                                 finish(i * 2 + (s0 + k - 2), (s0 + k) % 2, i * 2 + (m0 + k - 2)))
                    position += 2 * pairs
                    finished = position - 2
            finish_to(finished, T)

        @block.tensor
        def _(pe):
            pe.wait_ge(consts, 1)

            def product(n, odd):
                pe.wait_ge(scaled_t_ready, n + 1)
                at_least(pe, e_ready, n)
                return nc.tensor.matmul(prep[:, P:P + D], scaled_t[:, odd, :], w_both[:], start=True, stop=True)

            def flip_scaled(n, odd):
                pe.wait_ge(scaled_ready, n + 1)
                at_least(pe, scaled_t_ready, n)
                return nc.tensor.transpose(prep[:, 0:P], scaled[:, odd].rearrange("p h d -> p (h d)"), ident[:])

            flip_scaled(0, 0).then_inc(prep_ready, 1)
            pe.wait_ge(w_ready, 1)
            product(0, 0)
            flip_scaled(1, 1).then_inc(prep_ready, 1)

            def add_tiles(i):
                for k in range(ITER):
                    n = i * ITER + k
                    static = isinstance(n, int)
                    slot = k % SLOTS
                    columns = work[:, slot, :].rearrange("p (g h c) -> p g h c", g=G, h=2)
                    pe.wait_ge(tile_in[slot], (i * (ITER // SLOTS) + (k // SLOTS + 1)) * 16)
                    pe.wait_ge(e_ready, n + 1)
                    for b in range(XB):
                        for h in range(2):
                            last = nc.tensor.matmul(v_sum[b][D * h:D * h + D, :].rearrange("d (g c) -> d g c", g=G),
                                                    e_tile[:, k % 2, :], columns[:, :, h, P * b:P * b + P],
                                                    start=static and n == 0, stop=static and n == T - 1)
                        if static and n == T - 1:
                            last.then_inc(v_summed, 1)
                        if b == 2 and not (static and n + 1 >= T):
                            ready = product(n + 1, (k + 1) % 2)
                            if not static or n + 2 < T:
                                ready = flip_scaled(n + 2, k % 2)
                            ready.then_inc(prep_ready, 1)
                    if k == CACHE_AT:
                        pe.wait_ge(blocked_act, i + 1)
                        pe.wait_ge(blocked_dve, i + 1)
                        for c in range(CG):
                            at_least(pe, cached_dve if c % 2 else cached_act, i * (CG // 2) + c // 2)
                            for q in range(4):
                                last = nc.tensor.transpose(flip[c % 2][:, P * q:P * q + P], blocked[:, 4 * c + q, :],
                                                           ident[:])
                            if c < CG - 1:
                                last.then_inc(flipped, 1)
                    if not (static and n == T - 1):
                        last.then_inc(tile_used, 1)

            iterations(pe, add_tiles)

            for b in range(XB):
                if b % 2:
                    pe.wait_ge(vt_dve, b // 2 + 1)
                    at_least(pe, v_dve, b // 2)
                else:
                    pe.wait_ge(vt_act, b // 2 + 1)
                    at_least(pe, v_act, b // 2)
                for q in range(QB):
                    last = nc.tensor.transpose(flip[b % 2][:, P * q:P * q + P], vt[:, b, q].rearrange("p g c -> p (g c)"),
                                               ident[:])
                last.then_inc(v_flipped, 1)
            pe.wait_ge(v_act, (XB + 1) // 2)
            pe.wait_ge(v_dve, XB // 2)

            def center_rows(s, odd):
                pe.wait_ge(h_t_ready, s + 1)
                at_least(pe, y_ready, s - 1)
                nc.tensor.matmul(centered[odd], h_t[:, odd, :], center[:], start=True, stop=True).then_inc(h_centered, 1)

            def add_blocks(s, odd, rows):
                at_least(pe, h_t_ready, s - 1)
                for j in range(J // 2):
                    for h in range(2):
                        last = nc.tensor.matmul(h_sum[odd][D * h:D * h + D, :], v[:, j // QB, j % QB, h, :],
                                                rows[:, h * (J // 2) + j, :], start=j == 0, stop=j == J // 2 - 1)
                    if j == CENTER_AFTER and not (isinstance(s, int) and s == 0):
                        center_rows(s - 1, 1 - odd)
                last.then_inc(h_summed, 1)

            def add_streamed(s, odd, m, b):
                pe.wait_ge(run_turned, (m + 1) * A)
                add_blocks(s, odd, turned[:, b])

            position = 0
            for step in PLAN:
                if step[0] == "cached":
                    pe.wait_ge(cached_act, CACHED * CG // 2)
                    pe.wait_ge(cached_dve, CACHED * CG // 2)
                    add_blocks(position, position % 2, cache[:, step[1]])
                    position += 1
                elif step[0] == "single":
                    add_streamed(position, position % 2, step[1], step[1] % 2)
                    position += 1
                else:
                    _, m0, pairs = step
                    s0 = position
                    with pe.Fori(0, pairs) as i:
                        for k in range(2):
                            add_streamed(i * 2 + (s0 + k), (s0 + k) % 2, i * 2 + (m0 + k), k)
                    position += 2 * pairs
            center_rows(T - 1, 1)


INPUTS = ['x', 'adj', 'L0_gnn_W_u', 'L0_gnn_diag_u', 'L0_gnn_par_u', 'L0_gnn_W_i', 'L0_gnn_diag_i', 'L0_gnn_par_i',
          'L0_gnn_ln_gamma', 'L0_gnn_ln_beta']


def kernel(**inputs):
    import numpy as np
    import concourse.bacc as bacc
    from concourse.bass_utils import run_bass_kernel_spmd

    nc = bacc.Bacc("TRN2", target_bir_lowering=False, num_devices=1)
    arrays, args = {}, []
    for name in INPUTS:
        a = np.ascontiguousarray(inputs[name])
        arrays[name + "_dram"] = a
        args.append(nc.dram_tensor(name + "_dram", a.shape, mybir.dt.from_np(a.dtype), kind="ExternalInput").ap())
    out = nc.dram_tensor("out_dram", inputs['x'].shape, F32, kind="ExternalOutput").ap()
    build(nc, *args, out)
    return run_bass_kernel_spmd(nc, [arrays], core_ids=[0]).results[0]["out_dram"]
```

```python
from contextlib import ExitStack

import concourse.bass as bass
from concourse import mybir

F32 = mybir.dt.float32
U32 = mybir.dt.uint32
ALU = mybir.AluOpType
ACT = mybir.ActivationFunctionType
AX_X = mybir.AxisListType.X

P = 128
EPS = 1e-5

G = 4
SQ = 32


def build(nc, x, adj, W_u, diag_u, par_u, W_i, diag_i, par_i, ln_gamma, ln_beta, out):
    N, D = x.shape
    T = N // P
    NU = diag_u.shape[0]
    RUN = N // G
    HALF = RUN // 2
    XB = HALF // P
    QB = P // SQ
    J = RUN // SQ
    A = P // SQ
    assert G * RUN == N and XB * P == HALF and 2 * D == P and XB == 5

    CACHED = 5
    STREAMED = T - CACHED - 1
    RETAINED = STREAMED
    ITER = T // CACHED
    CACHE_AT = 3
    SLOTS = 4
    LAST_SLOTS = [0, 1, 2, 3, 1, 2, 3, 1]
    assert ITER * CACHED == T and ITER % SLOTS == 0 and len(LAST_SLOTS) == ITER and STREAMED % 2 == 0
    CENTER_AFTER = 3
    CG = J // 4

    X_ORDER = [0, CACHED - 1, *range(1, CACHED - 1)]

    PLAN = [("retained",), ("pairs", 0, 4), ("cached", 0), ("cached", 1), ("pairs", 8, 4), ("cached", 2), ("cached", 3),
            ("pairs", 16, 4), ("cached", 4), ("pairs", 24, 4), ("parts", STREAMED - 2)]
    ORDER = []
    for step in PLAN:
        if step[0] == "retained":
            ORDER.append(RETAINED)
        elif step[0] == "cached":
            ORDER.append(T - CACHED + step[1])
        else:
            ORDER += range(step[1], step[1] + (2 * step[2] if step[0] == "pairs" else 2))
    assert sorted(ORDER) == list(range(T)) and PLAN[-1] == ("parts", STREAMED - 2)

    with ExitStack() as ctx:
        def sb(name, shape, dt=F32):
            return ctx.enter_context(nc.sbuf_tensor(name, shape, dt))

        def bank(name):
            return ctx.enter_context(nc.psum_tensor(name, [P, 512], F32))

        def sem(name):
            return ctx.enter_context(nc.semaphore(name))

        work = sb("work", [P, SLOTS, N])
        cache = sb("cache", [P, CACHED, J, P])
        hv = sb("hv", [P, T, D])
        xr = sb("xr", [P, T, D])
        ident = sb("ident", [P, P])
        center = sb("center", [P, D])
        w_both = sb("w_both", [P, D])
        par = sb("par", [P, 2])
        diag = sb("diag", [P, 2, T])
        gamma = sb("gamma", [P, D])
        beta = sb("beta", [P, D])
        small = sb("small", [P, 2, 512])
        e_tile = sb("e_tile", [P, 2, D])
        stat = sb("stat", [P, 3, T])
        ssq = sb("ssq", [P, 2])
        std = sb("std", [P, 2])
        rstd = sb("rstd", [P, 2])
        eps = sb("eps", [P, 1])
        two_tiles = sb("two_tiles", [P, 1], U32)
        run_at = sb("run_at", [P, 2, A], U32)
        part_at = sb("part_at", [P, 2, 2, A], U32)

        scaled = small[:, 0, 0:256].rearrange("p (b h d) -> p b h d", b=2, h=2)
        scaled_t = small[:, 0, 256:512].rearrange("p (b r) -> p b r", b=2)
        h_t = small[:, 1, 0:256].rearrange("p (b r) -> p b r", b=2)
        z = small[:, 1, 256:256 + 2 * D].rearrange("p (b d) -> p b d", b=2)
        square = small[:, 1, 256 + 2 * D:256 + 3 * D]
        vt = small[:].rearrange("p b (q g c) -> p b q g c", q=QB, g=G)

        turned = [work[:, 1 - b, :].rearrange("p (j r) -> p j r", r=P) for b in range(2)]
        gathered = work[:, 2:4, :].rearrange("p b (a c) -> p b a c", a=A)
        v = hv[:].rearrange("p t d -> p (t d)").rearrange("p (b q h d) -> p b q h d", b=XB, q=QB, h=2)
        blocked = cache[:, CACHED - 1]
        sq_x = cache[:, 0, :, :].rearrange("p j r -> p (j r)")[:, 0:T * D].rearrange("p (t d) -> p t d", d=D)

        v_sum = [bank(f"v_sum{b}") for b in range(XB)]
        flip = [bank(f"flip{b}") for b in range(2)]
        prep = bank("prep")
        h_sum = [f[:, 0:P] for f in flip]
        centered = [v_sum[b][:, 0:D] for b in range(2)]

        x_in = [sem(f"x_in{c}") for c in range(CACHED)]
        w_in = sem("w_in")
        diag_in = sem("diag_in")
        norm_in = sem("norm_in")
        tile_in = [sem(f"tile_in{s}") for s in range(SLOTS)]
        diag_zero = sem("diag_zero")
        eps_ready = sem("eps_ready")
        consts = sem("consts")
        pool_step = sem("pool_step")
        xr_ready = sem("xr_ready")
        index_step = sem("index_step")
        index_ready = sem("index_ready")
        gathers_due = sem("gathers_due")
        dve_step = sem("dve_step")
        x_centered = sem("x_centered")
        x_squared = sem("x_squared")
        x_var = sem("x_var")
        x_std = sem("x_std")
        res_ready = sem("res_ready")
        w_ready = sem("w_ready")
        scaled_ready = sem("scaled_ready")
        prep_ready = sem("prep_ready")
        scaled_t_ready = sem("scaled_t_ready")
        e_ready = sem("e_ready")
        tile_used = sem("tile_used")
        blocked_act = sem("blocked_act")
        blocked_dve = sem("blocked_dve")
        flipped = sem("flipped")
        kept_act = sem("kept_act")
        kept_dve = sem("kept_dve")
        v_summed = sem("v_summed")
        vt_act = sem("vt_act")
        vt_dve = sem("vt_dve")
        v_flipped = sem("v_flipped")
        v_act = sem("v_act")
        v_dve = sem("v_dve")
        run_in = [[sem(f"run_in{b}{a}") for a in range(A)] for b in range(2)]
        rest_in = [[sem(f"rest_in{b}{a}") for a in range(A)] for b in range(2)]
        run_turned = sem("run_turned")
        h_summed = sem("h_summed")
        h_t_ready = sem("h_t_ready")
        h_centered = sem("h_centered")
        h_squared = sem("h_squared")
        std_ready = sem("std_ready")
        fin_step = sem("fin_step")
        y_ready = sem("y_ready")
        stored = sem("stored")

        adj_tiles = adj.rearrange("(p t) c -> t p c", t=T)
        adj_runs = adj.rearrange("r (g c) -> (r g) c", g=G)
        adj_parts = adj.rearrange("r (g c) -> (r g) c", g=2 * G)
        x_rows = x.rearrange("(p t) d -> p t d", t=T)
        out_rows = out.rearrange("(p t) d -> p t d", t=T)

        def at_least(eng, s, count):
            if not isinstance(count, int) or count > 0:
                eng.wait_ge(s, count)

        def tile_of(i, k):
            if k >= ITER:
                i, k = i + 1, k - ITER
            if k == CACHE_AT:
                return i + (T - CACHED)
            if k == 0:
                return i * (ITER - 1) + (ITER - 2)
            return i * (ITER - 1) + (k - 1 if k < CACHE_AT else k - 2)

        def is_last(i):
            return isinstance(i, int) and i == CACHED - 1

        def slot_of(i, k):
            return LAST_SLOTS[k] if is_last(i) else k % SLOTS

        def loads_of_slot(i, k):
            if is_last(i):
                return i * (ITER // SLOTS) + LAST_SLOTS[:k + 1].count(LAST_SLOTS[k])
            return i * (ITER // SLOTS) + (k // SLOTS + 1)

        def kept_number(i, k):
            if is_last(i) and k == 0:
                return CACHED - 1
            if k == CACHE_AT:
                return CACHED if is_last(i) else i
            return None

        def kept_blocks(i, k):
            return cache[:, i] if k == CACHE_AT else work[:, LAST_SLOTS[0], :].rearrange("p (j r) -> p j r", r=P)

        def blocks_free(i, k):
            n = i * ITER + k
            if is_last(i):
                return n - (ITER - CACHE_AT) + 1 if k == 0 else n - CACHE_AT + 1
            return n - ITER + 1

        def iterations(eng, body):
            body(0)
            with eng.Fori(1, CACHED - 1) as i:
                body(i)
            body(CACHED - 1)

        def copy_to_blocks(eng, copy, i, k, first, done):
            at_least(eng, tile_used, blocks_free(i, k))
            eng.wait_ge(tile_in[slot_of(i, k)], loads_of_slot(i, k) * 16)
            for g in range(first, G, 2):
                last = copy(blocked[:, :, SQ * g:SQ * g + SQ],
                            work[:, slot_of(i, k), RUN * g:RUN * g + RUN].rearrange("p (j c) -> p j c", c=SQ))
            last.then_inc(done, 1)

        def keep_blocks(eng, copy, i, k, parity, done):
            kept = kept_number(i, k)
            for c in range(parity, CG, 2):
                if c < CG - 1:
                    eng.wait_ge(flipped, kept * (CG - 1) + c + 1)
                else:
                    eng.wait_ge(tile_used, i * ITER + k + 1)
                copy(kept_blocks(i, k)[:, 4 * c:4 * c + 4, :].rearrange("p j r -> p (j r)"),
                     flip[parity][:]).then_inc(done, 1)

        def take_v(eng, copy, parity, vt_done, v_done):
            for b in range(parity, XB, 2):
                eng.wait_ge(v_summed, b + 1)
                at_least(eng, v_flipped, b - 1)
                copy(vt[:, parity].rearrange("p q g c -> p g q c"),
                     v_sum[b][:].rearrange("p (g q c) -> p g q c", g=G, q=QB)).then_inc(vt_done, 1)
                if b == parity:
                    eng.wait_ge(xr_ready, CACHED)
                else:
                    take_v_blocks(eng, copy, b - 2, v_done)
            take_v_blocks(eng, copy, b, v_done)

        def take_v_blocks(eng, copy, b, v_done):
            eng.wait_ge(v_flipped, b + 1)
            copy(v[:, b].rearrange("p q h d -> p (q h d)"), flip[b % 2][:]).then_inc(v_done, 1)

        def row_of(vector):
            return vector.rearrange("(a n) -> a n", a=1)

        def part_of(c):
            return slice(ITER * c, ITER * c + ITER)

        def load_x(eng, c):
            eng.dma_start(xr[:, part_of(c), :], x_rows[:, part_of(c), :]).then_inc(x_in[c], 16)

        block = ctx.enter_context(nc.Block())

        @block.sync
        def _(sp):
            load_x(sp, X_ORDER[0])

            def load(i):
                for k in range(ITER):
                    n = i * ITER + k
                    at_least(sp, tile_used, n - SLOTS + (2 if is_last(i) and k >= SLOTS else 1))
                    sp.dma_start(work[:, slot_of(i, k), :], adj_tiles[tile_of(i, k)]).then_inc(tile_in[slot_of(i, k)], 16)
                    if isinstance(n, int) and n == 0:
                        sp.dma_start(w_both[0:D, :], W_u).then_inc(w_in, 16)
                        sp.dma_start(w_both[D:P, :], W_i).then_inc(w_in, 16)
                        for c in X_ORDER[1:]:
                            load_x(sp, c)
                    if isinstance(n, int) and n == 1:
                        sp.dma_start(gamma[:], row_of(ln_gamma).to_broadcast([P, D])).then_inc(norm_in, 16)
                        sp.dma_start(beta[:], row_of(ln_beta).to_broadcast([P, D])).then_inc(norm_in, 16)

            iterations(sp, load)

            stores = 0

            def store(finished, first, end):
                sp.wait_ge(y_ready, finished)
                sp.dma_start(out_rows[:, first:end, :], xr[:, first:end, :]).then_inc(stored, 16)
                return 1

            position = 0
            for step in PLAN:
                if step[0] == "parts":
                    stores += store(T, step[1], step[1] + 2)
                elif step[0] != "pairs":
                    position += 1
                    if step[0] == "cached" and step[1] == CACHED - 1:
                        stores += store(position, RETAINED, T)
                else:
                    _, m0, pairs = step
                    position += 2 * pairs
                    stores += store(position, m0, m0 + 2 * pairs)
            sp.wait_ge(stored, 16 * stores)

        @block.gpsimd
        def _(pool):
            nc.gpsimd.memset(diag[:], 0.0).then_inc(diag_zero, 1)
            nc.gpsimd.memset(eps[:], EPS).then_inc(eps_ready, 1)
            nc.gpsimd.memset(ident[:], 0.0)
            nc.gpsimd.memset(center[:], -1.0 / D).then_inc(pool_step, 1)
            pool.wait_ge(pool_step, 1)
            nc.gpsimd.affine_select(out=ident[:], in_=ident[:], compare_op=ALU.not_equal, fill=1.0, base=0,
                                    pattern=[[-1, P]], channel_multiplier=1)
            nc.gpsimd.affine_select(out=center[:], in_=center[:], compare_op=ALU.not_equal, fill=1.0 - 1.0 / D,
                                    base=0, pattern=[[-1, D]], channel_multiplier=1).then_inc(pool_step, 1)
            pool.wait_ge(pool_step, 2)
            nc.gpsimd.affine_select(out=center[:], in_=center[:], compare_op=ALU.not_equal, fill=1.0 - 1.0 / D,
                                    base=-D, pattern=[[-1, D]], channel_multiplier=1).then_inc(consts, 1)
            pool.wait_ge(consts, 1)
            for g in range(G):
                nc.gpsimd.iota(run_at[SQ * g:SQ * g + SQ], pattern=[[G, 2], [SQ * T * G, A]], base=g,
                               channel_multiplier=T * G).then_inc(index_step, 1)
                nc.gpsimd.iota(part_at[SQ * g:SQ * g + SQ], pattern=[[2 * G, 2], [1, 2], [SQ * T * 2 * G, A]],
                               base=2 * g + (STREAMED - 2) * 2 * G, channel_multiplier=T * 2 * G).then_inc(index_step, 1)
                pool.wait_ge(index_step, 2 * g + 2)
            nc.gpsimd.iota(two_tiles[:], pattern=[[0, 1]], base=2 * G, channel_multiplier=0).then_inc(index_ready, 1)

            pool.wait_ge(norm_in, 2 * 16)
            beta_all = beta[:].rearrange("p (a d) -> p a d", a=1).to_broadcast([P, ITER, D])
            for count, c in enumerate(X_ORDER):
                chunk = xr[:, part_of(c), :]
                pool.wait_ge(res_ready, count + 1)
                nc.gpsimd.tensor_tensor(chunk, chunk, hv[:, part_of(c), :], ALU.add).then_inc(pool_step, 1)
                pool.wait_ge(pool_step, 3 + count)
                nc.gpsimd.tensor_tensor(chunk, chunk, beta_all, ALU.add).then_inc(xr_ready, 1)

            def gather(b, a):
                nc.gpsimd.indirect_dma_start(
                    out=gathered[:, b, a, :], out_offset=None, in_=adj_runs,
                    in_offset=bass.IndirectOffsetOnAxis(ap=run_at[:, b, a:a + 1], axis=0),
                ).then_inc(run_in[b][a], 16)

            def gather_part(b, a, part):
                nc.gpsimd.indirect_dma_start(
                    out=gathered[:, b, a, part * HALF:part * HALF + HALF], out_offset=None, in_=adj_parts,
                    in_offset=bass.IndirectOffsetOnAxis(ap=part_at[:, b, part, a:a + 1], axis=0),
                ).then_inc((rest_in if part else run_in)[b][a], 16)

            pool.wait_ge(index_ready, 1)
            pool.wait_ge(tile_used, T - 2)
            for a in range(A):
                gather(0, a)
            pool.wait_ge(tile_used, T - 1)
            for a in range(A):
                gather(1, a)

            with pool.Fori(1, STREAMED // 2 - 1) as i:
                for b in range(2):
                    for a in range(A):
                        count = i * (2 * A) + (b * A + a)
                        pool.wait_ge(run_turned, count - (2 * A - 1))
                        nc.gpsimd.tensor_tensor(run_at[:, b, a:a + 1], run_at[:, b, a:a + 1], two_tiles[:],
                                                ALU.add).then_inc(index_ready, 1)
                        pool.wait_ge(index_ready, count - (2 * A - 2))
                        pool.sem_inc(gathers_due, 1)
                        gather(b, a)
            for b in range(2):
                for a in range(A):
                    pool.wait_ge(run_turned, (STREAMED - 4 + b) * A + a + 1)
                    gather_part(b, a, 0)
                for a in range(A):
                    gather_part(b, a, 1)

        @block.scalar
        def _(act):
            full, rest = NU // T, NU % T
            act.wait_ge(diag_zero, 1)
            act.dma_start(diag[0:full, 0, :], diag_u[0:full * T].rearrange("(p t) -> p t", t=T)).then_inc(diag_in, 16)
            act.dma_start(diag[full:full + 1, 0, 0:rest], row_of(diag_u[full * T:NU])).then_inc(diag_in, 16)
            act.dma_start(diag[full:full + 1, 1, rest:T], row_of(diag_i[0:T - rest])).then_inc(diag_in, 16)
            act.dma_start(diag[full + 1:P, 1, :],
                           diag_i[T - rest:N - NU].rearrange("(p t) -> p t", t=T)).then_inc(diag_in, 16)
            act.dma_start(par[0:D, :], row_of(par_u).to_broadcast([D, 2])).then_inc(w_in, 16)
            act.dma_start(par[D:P, :], row_of(par_i).to_broadcast([D, 2])).then_inc(w_in, 16)
            act.wait_ge(eps_ready, 1)
            nc.scalar.activation(std[:, 0:1], eps[:], ACT.Sqrt)
            for count, c in enumerate(X_ORDER):
                part = part_of(c)
                act.wait_ge(x_centered, count + 1)
                nc.scalar.activation(sq_x[:, part, :], hv[:, part, :], ACT.Square).then_inc(x_squared, 1)
                act.wait_ge(x_var, count + 1)
                nc.scalar.activation(stat[:, 1, part], stat[:, 0, part], ACT.Sqrt, bias=eps[:],
                                     scale=1.0 / D).then_inc(x_std, 1)

            def keep(i):
                for k in range(ITER):
                    if kept_number(i, k) is not None:
                        copy_to_blocks(act, nc.scalar.copy, i, k, 0, blocked_act)
                        keep_blocks(act, nc.scalar.copy, i, k, 0, kept_act)

            iterations(act, keep)
            take_v(act, nc.scalar.copy, 0, vt_act, v_act)

            def spread(s, odd):
                act.wait_ge(h_centered, s + 1)
                at_least(act, y_ready, s - 1)
                nc.scalar.activation(square[:], centered[odd], ACT.Square,
                                     accum_out=ssq[:, odd:odd + 1]).then_inc(h_squared, 1)
                act.wait_ge(h_squared, s + 1)
                nc.scalar.activation(std[:, odd:odd + 1], ssq[:, odd:odd + 1], ACT.Sqrt, bias=eps[:],
                                     scale=1.0 / D).then_inc(std_ready, 1)

            def take_sum(s, odd):
                act.wait_ge(h_summed, s + 1)
                at_least(act, h_centered, s - 1)
                nc.scalar.copy(h_t[:, odd, :], h_sum[odd]).then_inc(h_t_ready, 1)

            take_sum(0, 0)
            spread(0, 0)
            take_sum(1, 1)
            with act.Fori(1, T // 2) as i:
                spread(i * 2 - 1, 1)
                take_sum(i * 2, 0)
                spread(i * 2, 0)
                take_sum(i * 2 + 1, 1)
            spread(T - 1, 1)

        @block.vector
        def _(dve):
            def make_res(count):
                part = part_of(X_ORDER[count])

                def spread_out(s):
                    return stat[:, s, part].rearrange("p (t a) -> p t a", a=1).to_broadcast([P, ITER, D])

                dve.wait_ge(x_in[X_ORDER[count]], 16)
                nc.vector.tensor_reduce(stat[:, 0, part], xr[:, part, :], AX_X, ALU.add).then_inc(dve_step, 1)
                dve.wait_ge(dve_step, 3 * count + 1)
                nc.vector.tensor_scalar(stat[:, 0, part], stat[:, 0, part], 1.0 / D, None, ALU.mult).then_inc(dve_step, 1)
                dve.wait_ge(dve_step, 3 * count + 2)
                nc.vector.tensor_tensor(hv[:, part, :], xr[:, part, :], spread_out(0),
                                        ALU.subtract).then_inc(x_centered, 1)
                dve.wait_ge(x_squared, count + 1)
                nc.vector.tensor_reduce(stat[:, 0, part], sq_x[:, part, :], AX_X, ALU.add).then_inc(x_var, 1)
                dve.wait_ge(x_std, count + 1)
                nc.vector.reciprocal(stat[:, 2, part], stat[:, 1, part]).then_inc(dve_step, 1)
                dve.wait_ge(dve_step, 3 * count + 3)
                nc.vector.scalar_tensor_tensor(out=hv[:, part, :], in0=hv[:, part, :], scalar=0.0, in1=spread_out(2),
                                               op0=ALU.max, op1=ALU.mult).then_inc(res_ready, 1)

            make_res(0)
            dve.wait_ge(w_in, 4 * 16)
            nc.vector.tensor_scalar(w_both[:], w_both[:], par[:, 0:1], par[:, 1:2], ALU.mult,
                                    ALU.mult).then_inc(w_ready, 1)
            dve.wait_ge(diag_in, 4 * 16)
            dve.wait_ge(res_ready, 1)

            def scale(t, n, odd):
                at_least(dve, prep_ready, n - 1)
                nc.vector.tensor_scalar(scaled[:, odd, 0, :], hv[:, t, :], diag[:, 0, bass.ds(t, 1)], None, ALU.mult)
                nc.vector.tensor_scalar(scaled[:, odd, 1, :], hv[:, t, :], diag[:, 1, bass.ds(t, 1)], None,
                                        ALU.mult).then_inc(scaled_ready, 1)

            def take_e(t, n, odd):
                dve.wait_ge(prep_ready, n + 2)
                at_least(dve, tile_used, n - 1)
                nc.vector.tensor_tensor(e_tile[:, odd, :], prep[:, P:P + D], hv[:, t, :], ALU.add).then_inc(e_ready, 1)

            def take_scaled_t(n, odd):
                dve.wait_ge(prep_ready, n + 1)
                nc.vector.tensor_copy(scaled_t[:, odd, :], prep[:, 0:P]).then_inc(scaled_t_ready, 1)

            scale(tile_of(0, 0), 0, 0)
            scale(tile_of(0, 1), 1, 1)
            take_scaled_t(0, 0)
            take_e(tile_of(0, 0), 0, 0)
            take_scaled_t(1, 1)
            make_res(1)
            dve.wait_ge(res_ready, 2)

            def prepare(i):
                for k in range(ITER):
                    n = i * ITER + k
                    static = isinstance(n, int)
                    if not static or n + 2 < T:
                        scale(tile_of(i, k + 2), n + 2, k % 2)
                    if not static or n + 1 < T:
                        take_e(tile_of(i, k + 1), n + 1, (k + 1) % 2)
                    if not static or n + 2 < T:
                        take_scaled_t(n + 2, k % 2)
                    if static and n < CACHED - 2:
                        make_res(n + 2)
                        dve.wait_ge(res_ready, n + 3)
                    if kept_number(i, k) is not None:
                        copy_to_blocks(dve, nc.vector.tensor_copy, i, k, 1, blocked_dve)
                        keep_blocks(dve, nc.vector.tensor_copy, i, k, 1, kept_dve)

            iterations(dve, prepare)
            take_v(dve, nc.vector.tensor_copy, 1, vt_dve, v_dve)

            def finish_step(step, s, odd, t):
                if step == 0:
                    dve.wait_ge(std_ready, s + 1)
                    nc.vector.reciprocal(rstd[:, odd:odd + 1], std[:, odd:odd + 1]).then_inc(fin_step, 1)
                elif step == 1:
                    dve.wait_ge(fin_step, s * 2 + 1)
                    nc.vector.scalar_tensor_tensor(out=z[:, odd, :], in0=centered[odd], scalar=rstd[:, odd:odd + 1],
                                                   in1=gamma[:], op0=ALU.mult, op1=ALU.mult).then_inc(fin_step, 1)
                else:
                    dve.wait_ge(fin_step, s * 2 + 2)
                    nc.vector.tensor_tensor(xr[:, t, :], xr[:, t, :], z[:, odd, :], ALU.add).then_inc(y_ready, 1)

            def turn(b, count, used, finishing):
                if isinstance(count, int) and count == 1 and b == 0:
                    dve.wait_ge(v_summed, XB)
                at_least(dve, h_summed, used)
                for a in range(A):
                    dve.wait_ge(run_in[b][a], count * 16)
                    nc.vector.transpose(turned[b][:, :, SQ * a:SQ * a + SQ],
                                        gathered[:, b, a, :].rearrange("p (j c) -> p j c", c=SQ)).then_inc(run_turned, 1)
                    if a > 0 and finishing:
                        finish_step(a - 1, *finishing)

            def turn_parts(b, used, finishing):
                dve.wait_ge(h_summed, used)
                for part, arrived, count in ((0, run_in, STREAMED // 2), (1, rest_in, 1)):
                    for a in range(A):
                        dve.wait_ge(arrived[b][a], count * 16)
                        nc.vector.transpose(
                            turned[b][:, part * (J // 2):(part + 1) * (J // 2), SQ * a:SQ * a + SQ],
                            gathered[:, b, a, part * HALF:part * HALF + HALF].rearrange("p (j c) -> p j c", c=SQ),
                        ).then_inc(run_turned, 1)
                        if part == 0 and a > 0:
                            finish_step(a - 1, *finishing)

            def summed_with(m):
                return 0 if m < -1 else ORDER.index(m if m >= 0 else RETAINED) + 1

            def at_position(s):
                return s, s % 2, ORDER[s]

            def finish_to(s, end):
                for p in range(s, end):
                    for step in range(3):
                        finish_step(step, *at_position(p))

            dve.wait_ge(norm_in, 2 * 16)
            position = 0
            finished = 0
            for step in PLAN:
                if step[0] == "parts":
                    for k in range(2):
                        turn_parts(k, summed_with(step[1] + k - 2), at_position(finished))
                        finished += 1
                elif step[0] != "pairs":
                    position += 1
                else:
                    _, m0, pairs = step
                    for k in range(2):
                        late = m0 > 0
                        turn(k, m0 // 2 + 1, summed_with(m0 + k - 2), at_position(finished) if late else None)
                        finished += late
                    finish_to(finished, position)
                    s0 = position
                    with dve.Fori(1, pairs) as i:
                        for k in range(2):
                            turn(k, i + (m0 // 2 + 1), i * 2 + (s0 + k - 1),
                                 (i * 2 + (s0 + k - 2), (s0 + k) % 2, i * 2 + (m0 + k - 2)))
                    position += 2 * pairs
                    finished = position - 2
            finish_to(finished, T)

        @block.tensor
        def _(pe):
            pe.wait_ge(consts, 1)

            def product(n, odd):
                pe.wait_ge(scaled_t_ready, n + 1)
                at_least(pe, e_ready, n)
                return nc.tensor.matmul(prep[:, P:P + D], scaled_t[:, odd, :], w_both[:], start=True, stop=True)

            def flip_scaled(n, odd):
                pe.wait_ge(scaled_ready, n + 1)
                at_least(pe, scaled_t_ready, n)
                return nc.tensor.transpose(prep[:, 0:P], scaled[:, odd].rearrange("p h d -> p (h d)"), ident[:])

            flip_scaled(0, 0).then_inc(prep_ready, 1)
            pe.wait_ge(w_ready, 1)
            product(0, 0)
            flip_scaled(1, 1).then_inc(prep_ready, 1)

            def add_tiles(i):
                for k in range(ITER):
                    n = i * ITER + k
                    static = isinstance(n, int)
                    columns = work[:, slot_of(i, k), :].rearrange("p (g h c) -> p g h c", g=G, h=2)
                    pe.wait_ge(tile_in[slot_of(i, k)], loads_of_slot(i, k) * 16)
                    pe.wait_ge(e_ready, n + 1)
                    for b in range(XB):
                        for h in range(2):
                            last = nc.tensor.matmul(v_sum[b][D * h:D * h + D, :].rearrange("d (g c) -> d g c", g=G),
                                                    e_tile[:, k % 2, :], columns[:, :, h, P * b:P * b + P],
                                                    start=static and n == 0, stop=static and n == T - 1)
                        if static and n == T - 1:
                            last.then_inc(v_summed, 1)
                        if b == 2 and not (static and n + 1 >= T):
                            ready = product(n + 1, (k + 1) % 2)
                            if not static or n + 2 < T:
                                ready = flip_scaled(n + 2, k % 2)
                            ready.then_inc(prep_ready, 1)
                    kept = kept_number(i, k)
                    if kept is not None:
                        pe.wait_ge(blocked_act, kept + 1)
                        pe.wait_ge(blocked_dve, kept + 1)
                        for c in range(CG):
                            at_least(pe, kept_dve if c % 2 else kept_act, kept * (CG // 2) + c // 2)
                            for q in range(4):
                                last = nc.tensor.transpose(flip[c % 2][:, P * q:P * q + P], blocked[:, 4 * c + q, :],
                                                           ident[:])
                            if c < CG - 1:
                                last.then_inc(flipped, 1)
                    if not (static and n == T - 1):
                        last.then_inc(tile_used, 1)

            iterations(pe, add_tiles)

            for b in range(XB):
                if b % 2:
                    pe.wait_ge(vt_dve, b // 2 + 1)
                    at_least(pe, v_dve, b // 2)
                else:
                    pe.wait_ge(vt_act, b // 2 + 1)
                    at_least(pe, v_act, b // 2)
                for q in range(QB):
                    last = nc.tensor.transpose(flip[b % 2][:, P * q:P * q + P],
                                               vt[:, b % 2, q].rearrange("p g c -> p (g c)"), ident[:])
                last.then_inc(v_flipped, 1)
            pe.wait_ge(v_act, (XB + 1) // 2)
            pe.wait_ge(v_dve, XB // 2)

            def center_rows(s, odd):
                pe.wait_ge(h_t_ready, s + 1)
                at_least(pe, y_ready, s - 1)
                nc.tensor.matmul(centered[odd], h_t[:, odd, :], center[:], start=True, stop=True).then_inc(h_centered, 1)

            def v_block(j):
                h, j = j // (J // 2), j % (J // 2)
                return v[:, j // QB, j % QB, h, :]

            def add_blocks(s, odd, rows, first=0, end=J):
                if first == 0:
                    at_least(pe, h_t_ready, s - 1)
                for j in range(first, end):
                    c = j % 2
                    last = nc.tensor.matmul(h_sum[odd][D * c:D * c + D, :], v_block(j), rows[:, j, :],
                                            start=j < 2, stop=j >= J - 2)
                    if j == 2 * CENTER_AFTER + 1 and not (isinstance(s, int) and s == 0):
                        center_rows(s - 1, 1 - odd)
                if end == J:
                    last.then_inc(h_summed, 1)

            def add_streamed(s, odd, m, b):
                pe.wait_ge(run_turned, (m + 1) * A)
                add_blocks(s, odd, turned[b])

            def add_parts(s, odd, m0, b):
                for part in range(2):
                    pe.wait_ge(run_turned, (m0 + 2 * b + part + 1) * A)
                    add_blocks(s, odd, turned[b], part * (J // 2), (part + 1) * (J // 2))

            position = 0
            for step in PLAN:
                if step[0] == "retained":
                    pe.wait_ge(kept_act, (CACHED + 1) * CG // 2)
                    pe.wait_ge(kept_dve, (CACHED + 1) * CG // 2)
                    add_blocks(position, position % 2, turned[1])
                    position += 1
                elif step[0] == "parts":
                    for k in range(2):
                        add_parts(position + k, (position + k) % 2, step[1], k)
                elif step[0] == "cached":
                    add_blocks(position, position % 2, cache[:, step[1]])
                    position += 1
                else:
                    _, m0, pairs = step
                    s0 = position
                    position += 2 * pairs
                    peeled = m0 == 0
                    for k in range(2 * peeled):
                        add_streamed(s0 + k, (s0 + k) % 2, m0 + k, k)
                    with pe.Fori(peeled, pairs) as i:
                        for k in range(2):
                            add_streamed(i * 2 + (s0 + k), (s0 + k) % 2, i * 2 + (m0 + k), k)
            center_rows(T - 1, 1)


INPUTS = ['x', 'adj', 'L0_gnn_W_u', 'L0_gnn_diag_u', 'L0_gnn_par_u', 'L0_gnn_W_i', 'L0_gnn_diag_i', 'L0_gnn_par_i',
          'L0_gnn_ln_gamma', 'L0_gnn_ln_beta']


def kernel(**inputs):
    import numpy as np
    import concourse.bacc as bacc
    from concourse.bass_utils import run_bass_kernel_spmd

    nc = bacc.Bacc("TRN2", target_bir_lowering=False, num_devices=1)
    arrays, args = {}, []
    for name in INPUTS:
        a = np.ascontiguousarray(inputs[name])
        arrays[name + "_dram"] = a
        args.append(nc.dram_tensor(name + "_dram", a.shape, mybir.dt.from_np(a.dtype), kind="ExternalInput").ap())
    out = nc.dram_tensor("out_dram", inputs['x'].shape, F32, kind="ExternalOutput").ap()
    build(nc, *args, out)
    return run_bass_kernel_spmd(nc, [arrays], core_ids=[0]).results[0]["out_dram"]
```
